# Optimizing a Trainium2 kernel written in Bass

```python
import numpy as np
import jax
import jax.numpy as jnp

def _softmax(x, axis=-1):
    return jax.nn.softmax(x, axis=axis)
def _gelu(x):
    return jax.nn.gelu(x, approximate=True)
def _silu(x):
    return jax.nn.silu(x)
def _sigmoid(x):
    return jax.nn.sigmoid(x)
def _layernorm(x, axis=-1, eps=1e-5):
    m = jnp.mean(x, axis=axis, keepdims=True)
    v = jnp.var(x, axis=axis, keepdims=True)
    return (x - m) / jnp.sqrt(v + eps)
def _scatter_add(tgt, idx, src, axis=0):
    return tgt.at[idx].add(src)
def _segment_sum(src, seg, n):
    return jax.ops.segment_sum(src, seg, n)

kernel_name = 'mk_adj_resnorm_d2_adj_128_b7fcee'

def setup_inputs(seed: int = 0):
    np.random.seed(seed)
    _w = jnp.asarray
    def _rec_inputs():
        import jax
        import jax.numpy as jnp
        _gk = jax.random.key(seed)
        x = -0.000929 + 1 * jax.random.normal(jax.random.fold_in(_gk, 1), (8192, 128), jnp.float32)
        _w = (1.0 + jnp.arange(8192, dtype=jnp.float32)) ** -0.5
        _w = _w / _w.mean()
        _pij = jnp.clip(0.000976562 * _w[:, None] * _w[None, :], 0.0, 1.0)
        _a = jax.random.uniform(jax.random.fold_in(_gk, 2), (8192, 8192)) < _pij
        _a = jnp.logical_or(_a, jnp.eye(8192, dtype=bool))
        _af = _a.astype(jnp.float32)
        adj = _af
        return x, adj
    x, adj = _rec_inputs()
    def _L0_gnn_setup():
        import jax, jax.numpy as jnp
        import numpy as np
        N = 8192
        DIN = 128
        F = 64
        H = 2
        NEG_BIG = -10000000000.0
        key = jax.random.key(seed)
        k1, k2, k3, k4 = jax.random.split(key, 4)
        x = jax.random.normal(k1, (N, DIN), dtype=jnp.float32)
        adj = (jax.random.uniform(k2, (N, N)) < 0.002).astype(jnp.float32)
        idx = jnp.arange(N)
        adj = adj.at[idx, idx].set(1.0)
        kernels = jax.random.normal(k3, (H, DIN, F), dtype=jnp.float32) * 0.05
        att_kernels = jax.random.normal(k4, (H, 2 * F), dtype=jnp.float32) * 0.05
        return {'x': x, 'adj': adj, 'kernels': kernels, 'att_kernels': att_kernels}
    _L0_gnn_all = _L0_gnn_setup()
    _L0_gnn_in = {k: v for k, v in _L0_gnn_all.items() if k in ('kernels', 'att_kernels', )}
    del _L0_gnn_all

    def _L1_gnn_setup():
        import jax, jax.numpy as jnp
        import numpy as np

        def _lap_mul(A, x):
            d = 1.0 / jnp.sqrt(jnp.sum(A, axis=-1))
            return d[:, None] * (A @ (d[:, None] * x))
        key = jax.random.key(seed)
        k1, k2, k3, k4, k5, k6 = jax.random.split(key, 6)
        N, D_IN, D_OUT = (4096, 128, 128)
        x = jax.random.normal(k1, (N, D_IN), dtype=jnp.float32)
        A = jax.random.uniform(k2, (N, N), dtype=jnp.float32)
        s1 = 1.0 / np.sqrt(D_IN)
        W1 = jax.random.uniform(k3, (D_IN, D_OUT), minval=-s1, maxval=s1, dtype=jnp.float32)
        b1 = jax.random.uniform(k4, (D_OUT,), minval=-s1, maxval=s1, dtype=jnp.float32)
        W2 = jax.random.uniform(k5, (D_IN, D_OUT), minval=-s1, maxval=s1, dtype=jnp.float32)
        b2 = jax.random.uniform(k6, (D_OUT,), minval=-s1, maxval=s1, dtype=jnp.float32)
        return {'x': x, 'A': A, 'W1': W1, 'b1': b1, 'W2': W2, 'b2': b2, 'sigma': 1, 'k': 4}
    _L1_gnn_all = _L1_gnn_setup()
    _L1_gnn_in = {k: v for k, v in _L1_gnn_all.items() if k in ('W1', 'b1', 'W2', 'b2', )}
    del _L1_gnn_all

    return {
        "x": x,
        "adj": adj,
        "L0_gnn_kernels": _L0_gnn_in["kernels"],
        "L0_gnn_att_kernels": _L0_gnn_in["att_kernels"],
        "L1_gnn_W1": _L1_gnn_in["W1"],
        "L1_gnn_b1": _L1_gnn_in["b1"],
        "L1_gnn_W2": _L1_gnn_in["W2"],
        "L1_gnn_b2": _L1_gnn_in["b2"],
    }

def reference(x, adj, L0_gnn_kernels, L0_gnn_att_kernels, L1_gnn_W1, L1_gnn_b1, L1_gnn_W2, L1_gnn_b2):
    import jax
    import jax.numpy as jnp
    def _L0_gnn_ref(x, adj, kernels, att_kernels):
        import jax, jax.numpy as jnp
        import numpy as np
        N = 8192
        DIN = 128
        F = 64
        H = 2
        NEG_BIG = -10000000000.0
        conv = jnp.einsum('nd,hdf->hnf', x, kernels)
        a_self = jnp.einsum('hnf,hf->hn', conv, att_kernels[:, :F])
        a_neigh = jnp.einsum('hnf,hf->hn', conv, att_kernels[:, F:])
        scores = jax.nn.elu(a_self[:, :, None] + a_neigh[:, None, :], alpha=1.0)
        mask = jnp.exp(adj * NEG_BIG) * NEG_BIG
        p = jax.nn.softmax(scores + mask[None, :, :], axis=-1)
        out = jnp.einsum('hnm,hmf->hnf', p, conv)
        return out.transpose(1, 0, 2).reshape(N, H * F)

    def _L1_gnn_ref(x, A, W1, b1, W2, b2, sigma, k):
        import jax, jax.numpy as jnp
        import numpy as np

        def _lap_mul(A, x):
            d = 1.0 / jnp.sqrt(jnp.sum(A, axis=-1))
            return d[:, None] * (A @ (d[:, None] * x))
        z = _lap_mul(A, x) @ W1 + b1
        z = jax.nn.leaky_relu(z, negative_slope=0.1)
        sq = jnp.sum(z * z, axis=-1)
        d2 = sq[:, None] + sq[None, :] - 2.0 * (z @ z.T)
        d2 = jnp.maximum(d2, 0.0)
        S = jnp.sqrt(d2 + 1e-10)
        S = jnp.exp(-S / (2.0 * sigma))
        order = jnp.argsort(-S, axis=-1)
        ranks = jnp.argsort(order, axis=-1)
        S = jnp.where(ranks < k, S, 0.0)
        A2 = S + A
        out = _lap_mul(A2, x) @ W2 + b2
        return out

    x = _layernorm(x + _L0_gnn_ref(x, adj, L0_gnn_kernels, L0_gnn_att_kernels), axis=-1)
    x = _layernorm(x + _L1_gnn_ref(x, adj, L1_gnn_W1, L1_gnn_b1, L1_gnn_W2, L1_gnn_b2, 1, 4), axis=-1)
    return x


_drawn_inputs = setup_inputs


def setup_inputs(seed=0):
    import zlib

    import numpy as np

    out = dict(_drawn_inputs(seed))
    spreads = {}
    factors = {}
    for name, (base, spread) in spreads.items():
        noise = np.random.default_rng([zlib.crc32(name.encode()), seed]).standard_normal(out[name].shape)
        drawn = base * np.exp(spread * noise) if base else spread * noise
        out[name] = jnp.asarray(drawn.astype(out[name].dtype))
    for name, factor in factors.items():
        out[name] = (out[name] * factor).astype(out[name].dtype)
    return out
```

```python
from contextlib import ExitStack

import numpy as np

import concourse.bass as bass
from concourse import mybir
from concourse.alu_op_type import AluOpType as ALU

ACT = mybir.ActivationFunctionType
AX_X = mybir.AxisListType.X
F32 = mybir.dt.float32
F16 = mybir.dt.float16
BF16 = mybir.dt.bfloat16
U32 = mybir.dt.uint32

P = 128
N = 8192
D = 128
H = 2
F = D // H
CH = 512
NB = CH // P
NC = N // CH
MT = N // P
WT = 4
NW = MT // WT
BODY = 2 * WT
PRIME = 8
NEIGHBOURS = 4
BIG = 2.0 ** 120
BOUND = 30.0
CAP = 80.0
YSCALE = 2.0 ** 11
EPS_LN = 1e-5
EPS_D2 = 1e-10
SLOPE = 0.1
LW = 8
NLW = MT // LW


def done(n):
    return PRIME + n


def resnorm_gnn_kernel(nc, x, adj, kernels, att, w1, b1, w2, b2, out):
    adj_t = nc.dram_tensor("adj_t", (NC, P, MT, CH), BF16).ap()
    y2_rows = nc.dram_tensor("y2_rows", (N, D), F32).ap()
    with ExitStack() as kept:
        x1 = kept.enter_context(nc.sbuf_tensor("x1", [P, MT, D], F32))
        deg = kept.enter_context(nc.sbuf_tensor("deg", [P, MT], F32))
        ident = kept.enter_context(nc.sbuf_tensor("ident", [P, P], F32))
        layer0(nc, x, adj, kernels, att, adj_t, x1, deg, ident)
        layer1(nc, w1, b1, w2, b2, adj_t, y2_rows, x1, deg, ident, out)


def layer0(nc, x, adj, kernels, att, adj_t, x1, deg, ident):
    with ExitStack() as ctx:
        def sb(name, shape, dt=F32):
            return ctx.enter_context(nc.sbuf_tensor(name, shape, dt))

        t = dict(
            self_row=sb("self_row", [P, H, N]),
            e_neigh=sb("e_neigh", [P, H, MT + 2]),
            score_col=sb("score_col", [P, 2 * H, MT + 2]),
            conv=sb("conv", [P, MT, H, F + 1]),
            ones=sb("ones", [P, P]),
            big_eye=sb("big_eye", [P, P], BF16),
            zero_bf=sb("zero_bf", [P, CH], BF16),
            one_bf=sb("one_bf", [P, 2], BF16),
            x_t=sb("x_t", [P, 2, CH]),
            w=sb("w", [P, 4, H, CH]),
            flag=sb("flag", [1, 1], U32),
        )
        project(nc, x, kernels, att, x1=x1, ident=ident, **t)
        attend(nc, adj, adj_t, x1=x1, deg=deg, ident=ident, **t)


def project(nc, x, kernels, att, x1, ident, self_row, e_neigh, score_col, conv, ones, big_eye, zero_bf,
            one_bf, x_t, w, flag):
    with ExitStack() as ctx:
        def sb(name, shape, dt=F32):
            return ctx.enter_context(nc.sbuf_tensor(name, shape, dt))

        def psum(name, shape):
            return ctx.enter_context(nc.psum_tensor(name, shape, F32))

        def sem(name):
            return ctx.enter_context(nc.semaphore(name))

        kcat = sb("kcat", [P, D])
        att_row = sb("att_row", [1, H * 2 * F])
        prod = sb("prod", [P, 2, H, F])
        w4 = sb("w4", [P, 2 * H])
        w_rep = sb("w_rep", [P, H, P])
        lim = sb("lim", [P, 2, NC + 1])
        edge = sb("edge", [P, 4])
        xin = w[:, 0].rearrange("p s (j d) -> p s j d", j=NB)

        turned = psum("turned", [P, 2, CH])
        conv_ps = psum("conv_ps", [P, 2, CH])
        rows_ps = psum("rows_ps", [P, H, CH])
        cols_ps = psum("cols_ps", [P, 2, CH])

        small_loaded = sem("small_loaded")
        const_made = sem("const_made")
        step_done = sem("step_done")
        att_spread = sem("att_spread")
        w_rep_made = sem("w_rep_made")
        x_loaded = [sem("x_loaded0"), sem("x_loaded1")]
        x1_loaded = sem("x1_loaded")
        x_turned = sem("x_turned")
        xt_copied = sem("xt_copied")
        cols_done = sem("cols_done")
        rows_done = sem("rows_done")
        conv_kept = sem("conv_kept")
        cols_kept = sem("cols_kept")
        exp_kept = sem("exp_kept")
        edge_done = sem("edge_done")
        flag_summed = sem("flag_summed")

        x_view = x.rearrange("(c j p) d -> c p j d", j=NB, p=P)
        block = ctx.enter_context(nc.Block())

        @block.sync
        def _(sp):
            sp.dma_start(kcat[:].rearrange("p (h f) -> p h f", h=H),
                         kernels.rearrange("h d f -> d h f")).then_inc(small_loaded, 16)
            sp.dma_start(att_row[:], att.rearrange("(a h) f -> a (h f)", a=1)).then_inc(small_loaded, 16)
            for s in range(2):
                sp.dma_start(xin[:, s], x_view[s]).then_inc(x_loaded[s], 16)
            sp.dma_start(x1[:], x.rearrange("(t p) d -> p t d", p=P)).then_inc(x1_loaded, 16)
            with sp.Fori(0, NC // 2 - 1) as g:
                for s in range(2):
                    sp.wait_ge(x_turned, 2 * g + s + 1)
                    sp.dma_start(xin[:, s], x_view[2 * g + s + 2]).then_inc(x_loaded[s], 16)
            sp.wait_ge(x1_loaded, 16)

        @block.gpsimd
        def _(pool):
            nc.gpsimd.memset(ones[:], 1.0).then_inc(const_made, 1)
            nc.gpsimd.memset(ident[:], 0.0).then_inc(const_made, 1)
            pool.wait_ge(const_made, 2)
            nc.gpsimd.affine_select(out=ident[:], in_=ident[:], compare_op=ALU.not_equal, fill=1.0,
                                    base=0, pattern=[[-1, P]], channel_multiplier=1).then_inc(const_made, 1)
            nc.gpsimd.memset(big_eye[:], 0.0).then_inc(const_made, 1)
            nc.gpsimd.memset(zero_bf[:], 0.0)
            nc.gpsimd.memset(one_bf[:], 1.0)
            nc.gpsimd.memset(conv[:, :, :, F:F + 1], 1.0)
            pool.wait_ge(const_made, 4)
            nc.gpsimd.affine_select(out=big_eye[:], in_=big_eye[:], compare_op=ALU.not_equal, fill=BIG,
                                    base=0, pattern=[[-1, P]], channel_multiplier=1).then_inc(const_made, 1)

        @block.tensor
        def _(pe):
            for s in (cols_done, rows_done):
                pe.sem_inc(s, PRIME)
            pe.wait_ge(const_made, 3)
            pe.wait_ge(small_loaded, 32)
            nc.tensor.matmul(cols_ps[:, 0, 0:2 * D], ones[0:1, :], att_row[0:1, :], start=True, stop=True) \
                .then_inc(att_spread, 1)
            pe.wait_ge(w_rep_made, 1)

            def turn(s, loads):
                pe.wait_ge(x_loaded[s], loads)
                for j in range(NB):
                    ins = nc.tensor.transpose(turned[:, s, j * P:(j + 1) * P], xin[:, s, j, :], ident[:])
                ins.then_inc(x_turned, 1)

            def products(c, s):
                pe.wait_ge(xt_copied, done(c + 1))
                pe.wait_ge(conv_kept, done(c - 1))
                for j in range(NB):
                    nc.tensor.matmul(conv_ps[:, s, j * P:(j + 1) * P], x_t[:, s, j * P:(j + 1) * P],
                                     kcat[:], start=True, stop=True)
                pe.wait_ge(cols_kept, done(c - 1))
                for j in range(NB):
                    ins = nc.tensor.matmul(cols_ps[:, s, j * 2 * H:(j + 1) * 2 * H], x_t[:, s, j * P:(j + 1) * P],
                                           w4[:], start=True, stop=True)
                ins.then_inc(cols_done, 1)
                pe.wait_ge(exp_kept, done(c))
                for h in range(H):
                    ins = nc.tensor.matmul(rows_ps[:, h, :], w_rep[:, h, :], x_t[:, s, :], start=True, stop=True)
                ins.then_inc(rows_done, 1)

            turn(0, 16)
            with pe.Fori(0, NC // 2 - 1) as g:
                turn(1, 16 * (g + 1))
                products(2 * g, 0)
                turn(0, 16 * (g + 2))
                products(2 * g + 1, 1)
            turn(1, 16 * (NC // 2))
            products(NC - 2, 0)
            products(NC - 1, 1)
            pe.wait_ge(exp_kept, done(NC))
            pe.wait_ge(edge_done, 1)
            nc.tensor.matmul(rows_ps[0:1, 0, 0:1], edge[:, 0:1], ones[:, 0:1], start=True, stop=True) \
                .then_inc(flag_summed, 1)

        @block.scalar
        def _(act):
            for s in (exp_kept, xt_copied):
                act.sem_inc(s, PRIME)

            def copy_xt(c, s):
                act.wait_ge(x_turned, c + 1)
                act.wait_ge(rows_done, done(c - 1))
                nc.scalar.activation(x_t[:, s, :], turned[:, s, :], ACT.Copy).then_inc(xt_copied, 1)

            def keep_rows(c):
                act.wait_ge(rows_done, done(c + 1))
                nc.scalar.activation(self_row[:, :, bass.ds(c * CH, CH)], rows_ps[:], ACT.Exp) \
                    .then_inc(exp_kept, 1)

            copy_xt(0, 0)
            with act.Fori(0, NC // 2 - 1) as g:
                copy_xt(2 * g + 1, 1)
                keep_rows(2 * g)
                copy_xt(2 * g + 2, 0)
                keep_rows(2 * g + 1)
            copy_xt(NC - 1, 1)
            keep_rows(NC - 2)
            keep_rows(NC - 1)
            act.wait_ge(cols_kept, done(NC + 1))
            nc.scalar.activation(e_neigh[:], score_col[:, H:2 * H, :], ACT.Exp).then_inc(exp_kept, 1)

        @block.vector
        def _(dve):
            steps = [0]

            def then(ins):
                steps[0] += 1
                ins.then_inc(step_done, 1)
                dve.wait_ge(step_done, steps[0])

            for s in (conv_kept, cols_kept):
                dve.sem_inc(s, PRIME)
            dve.wait_ge(att_spread, 1)
            dve.wait_ge(small_loaded, 32)
            att_ps = cols_ps[:, 0, 0:2 * D].rearrange("p (h a f) -> p a h f", h=H, a=2)
            for a in range(2):
                ins = nc.vector.tensor_tensor(prod[:, a], att_ps[:, a], kcat[:].rearrange("p (h f) -> p h f", h=H),
                                              ALU.mult)
            then(ins)
            then(nc.vector.tensor_reduce(w4[:], prod[:].rearrange("p a h f -> p (a h) f"), AX_X, ALU.add))
            for h in range(H):
                ins = nc.vector.tensor_scalar(w_rep[:, h, :], ones[:], w4[:, h:h + 1], None, ALU.mult)
            ins.then_inc(w_rep_made, 1)
            with dve.Fori(0, NC // 2) as g:
                for s in range(2):
                    c = 2 * g + s
                    dve.wait_ge(cols_done, done(c + 1))
                    nc.vector.tensor_copy(conv[:, bass.ds(c * NB, NB), :, 0:F],
                                          conv_ps[:, s, :].rearrange("p (j h f) -> p j h f", j=NB, h=H)) \
                        .then_inc(conv_kept, 1)
                    nc.vector.tensor_copy(score_col[:, :, bass.ds(c * NB, NB)],
                                          cols_ps[:, s, 0:NB * 2 * H].rearrange("p (j k) -> p k j", k=2 * H)) \
                        .then_inc(cols_kept, 1)
                    dve.wait_ge(exp_kept, done(c + 1))
                    for k, op in enumerate((ALU.max, ALU.min)):
                        nc.vector.tensor_reduce(lim[:, k, bass.ds(c, 1)], self_row[:, :, bass.ds(c * CH, CH)],
                                                mybir.AxisListType.XY, op)
            dve.wait_ge(cols_kept, done(NC))
            nc.vector.tensor_copy(score_col[:, :, MT:MT + 2], score_col[:, :, 0:2]).then_inc(cols_kept, 1)
            dve.wait_ge(exp_kept, done(NC + 1))
            for k, op in enumerate((ALU.max, ALU.min)):
                ins = nc.vector.tensor_reduce(lim[:, k, NC:NC + 1], e_neigh[:], mybir.AxisListType.XY, op)
            then(ins)
            for k, op in enumerate((ALU.max, ALU.min)):
                ins = nc.vector.tensor_reduce(edge[:, k:k + 1], lim[:, k, :], AX_X, op)
            then(ins)
            nc.vector.tensor_scalar(edge[:, 2:3], edge[:, 0:1], float(np.exp(BOUND)), None, ALU.is_gt)
            then(nc.vector.tensor_scalar(edge[:, 3:4], edge[:, 1:2], float(np.exp(-BOUND)), None, ALU.is_lt))
            nc.vector.tensor_tensor(edge[:, 0:1], edge[:, 2:3], edge[:, 3:4], ALU.add).then_inc(edge_done, 1)
            dve.wait_ge(flag_summed, 1)
            nc.vector.tensor_scalar(flag[:], rows_ps[0:1, 0, 0:1], 0.5, None, ALU.is_gt)


def attend(nc, adj, adj_t, x1, deg, ident, self_row, e_neigh, score_col, conv, ones, big_eye, zero_bf,
           one_bf, x_t, w, flag):
    with ExitStack() as ctx:
        def sb(name, shape, dt=F32):
            return ctx.enter_context(nc.sbuf_tensor(name, shape, dt))

        def psum(name, shape):
            return ctx.enter_context(nc.psum_tensor(name, shape, F32))

        def sem(name):
            return ctx.enter_context(nc.semaphore(name))

        adj_f = sb("adj_f", [P, 2, NB, WT * P])
        adj_m1 = sb("adj_m1", [P, 2, NB, WT * P], BF16)
        at = sb("at", [P, 2, WT, CH], BF16)
        u = sb("u", [P, 4, H, CH])
        conv_win = sb("conv_win", [P, 2, WT, H, F + 1])
        rden = sb("rden", [P, H, NB])
        row_top = sb("row_top", [P, H, NB])
        acc_sb = x_t[0:F + 1]

        mask = psum("mask", [P, 2, CH])
        acc = psum("acc", [P, 2, H, CH])
        fin = psum("fin", [P, 2, CH])
        FIN = NB * (F + 1)
        DEG = CH - NB

        adj_loaded = [sem("adj_loaded0"), sem("adj_loaded1")]
        win_loaded = [sem("win_loaded0"), sem("win_loaded1")]
        at_stored = [sem("at_stored0"), sem("at_stored1")]
        cast_done = sem("cast_done")
        gate = sem("gate")
        gate_dve = sem("gate_dve")
        gate_pe = sem("gate_pe")
        mask_done = sem("mask_done")
        raw_done = sem("raw_done")
        raised_done = sem("raised_done")
        u_done = sem("u_done")
        relu_done = sem("relu_done")
        exp_done = sem("exp_done")
        weight_done = sem("weight_done")
        sum_done = sem("sum_done")
        at_done = sem("at_done")
        deg_done = sem("deg_done")
        acc_copied = sem("acc_copied")
        turn_done = sem("turn_done")
        rden_done = sem("rden_done")
        fin_read = sem("fin_read")
        row_loaded = [sem("row_loaded0"), sem("row_loaded1")]
        row_cast = sem("row_cast")
        row_masked = sem("row_masked")
        row_max = sem("row_max")
        row_turned = sem("row_turned")
        col_step = sem("col_step")
        col_spread = sem("col_spread")
        row_spread = sem("row_spread")
        row_kept = sem("row_kept")

        adj_view = adj.rearrange("(c j p) (w m) -> c w p j m", j=NB, p=P, m=WT * P)
        GC = NW // 2
        LAST = NC * GC
        block = ctx.enter_context(nc.Block())

        @block.sync
        def _(sp):
            def find_maxima():
                with sp.Fori(0, LAST) as g:
                    for s in range(2):
                        sp.wait_ge(row_cast, done(2 * g + s - 1))
                        sp.dma_start(adj_f[:, s], adj_view[g // GC, (g % GC) * 2 + s]).then_inc(row_loaded[s], 16)
                sp.wait_ge(row_cast, done(2 * LAST))

            def weigh():
                for s in range(2):
                    sp.dma_start(adj_f[:, s], adj_view[0, s]).then_inc(adj_loaded[s], 16)
                    sp.dma_start(conv_win[:, s], conv[:, s * WT:(s + 1) * WT]).then_inc(win_loaded[s], 16)
                sp.wait_ge(cast_done, done(NB))
                sp.dma_start(adj_f[:, 0], adj_view[0, 2]).then_inc(adj_loaded[0], 16)
                with sp.Fori(0, LAST) as g:
                    for s in range(2):
                        win = 2 * g + s
                        nxt, nxt3, s3 = (g + 1) % LAST, (g + 1 + s) % LAST, (s + 1) % 2
                        sp.wait_ge(cast_done, done(NB * (win + 2)))
                        sp.dma_start(adj_f[:, s3], adj_view[nxt3 // GC, (nxt3 % GC) * 2 + s3]) \
                            .then_inc(adj_loaded[s3], 16)
                        sp.wait_ge(at_done, done(WT * (win + 1)))
                        sp.dma_start(adj_t[g // GC, :, bass.ds(((g % GC) * 2 + s) * WT, WT), :], at[:, s]) \
                            .then_inc(at_stored[s], 16)
                        sp.wait_ge(sum_done, done(WT * (win + 1)))
                        sp.dma_start(conv_win[:, s], conv[:, bass.ds((nxt % GC * 2 + s) * WT, WT)]) \
                            .then_inc(win_loaded[s], 16)
                for s in range(2):
                    sp.wait_ge(adj_loaded[s], 16 * (LAST + 2 - s))
                    sp.wait_ge(at_stored[s], 16 * (LAST + 1))
                    sp.wait_ge(win_loaded[s], 16 * (LAST + 1))

            beyond = sp.value_load(flag[0:1, 0:1], min_val=0, max_val=1)
            with sp.If(beyond == 1):
                find_maxima()
            weigh()

        @block.gpsimd
        def _(pool):
            for s in at_stored:
                pool.sem_inc(s, 16)
            for s in (cast_done, at_done, row_cast):
                pool.sem_inc(s, PRIME)

            def find_maxima():
                with pool.Fori(0, LAST) as g:
                    for s in range(2):
                        pool.wait_ge(row_loaded[s], 16 * (g + 1))
                        pool.wait_ge(row_masked, done(WT * (2 * g + s - 1)))
                        pool.sem_inc(gate, 1)
                        nc.gpsimd.tensor_scalar(adj_m1[:, s], adj_f[:, s], 1.0, -1.0, ALU.mult, ALU.add) \
                            .then_inc(row_cast, 1)
                pool.wait_ge(row_masked, done(WT * 2 * LAST))

            def cast(s, j):
                nc.gpsimd.tensor_scalar(adj_m1[:, s, j], adj_f[:, s, j], 1.0, -1.0, ALU.mult, ALU.add) \
                    .then_inc(cast_done, 1)

            def weigh():
                for s in range(2):
                    pool.wait_ge(adj_loaded[s], 16)
                    for j in range(NB):
                        cast(s, j)
                with pool.Fori(0, LAST) as g:
                    for s in range(2):
                        pool.wait_ge(at_stored[s], 16 * (g + 1))
                        pool.wait_ge(deg_done, done(WT * (2 * g + s - 1)))
                        for t in range(WT):
                            pool.wait_ge(weight_done, done((2 * g + s) * WT + t + 1))
                            pool.sem_inc(gate, 1)
                            nc.gpsimd.tensor_scalar(at[:, s, t, :], u[:, t, 0, :], 0.0, None, ALU.is_gt) \
                                .then_inc(at_done, 1)
                            if t == 0:
                                pool.wait_ge(adj_loaded[s], 16 * (g + 2))
                                pool.wait_ge(mask_done, done((2 * g + s + 1) * WT))
                                pool.sem_inc(gate, 1)
                            cast(s, t)

            beyond = pool.value_load(flag[0:1, 0:1], min_val=0, max_val=1)
            with pool.If(beyond == 1):
                find_maxima()
            weigh()

        @block.tensor
        def _(pe):
            for s in (mask_done, sum_done, deg_done, turn_done, row_masked, row_turned):
                pe.sem_inc(s, PRIME)

            def make_mask(slot, s, t):
                for j in range(NB):
                    ins = nc.tensor.matmul(mask[:, slot, j * P:(j + 1) * P], adj_m1[:, s, j, t * P:(t + 1) * P],
                                           big_eye[:], start=True, stop=True)
                return ins

            def find_maxima():
                with pe.Fori(0, NC) as c:
                    with pe.Fori(0, GC) as g:
                        for k in range(BODY):
                            unit = c * MT + g * BODY + k
                            pe.wait_ge(row_cast, done((c * GC + g) * 2 + k // WT + 1))
                            pe.wait_ge(row_max, done(unit - 1))
                            make_mask(k % 2, k // WT, k % WT).then_inc(row_masked, 1)
                    pe.wait_ge(row_max, done(MT * (c + 1)))
                    pe.wait_ge(row_kept, done(c))
                    for h in range(H):
                        for j in range(NB):
                            ins = nc.tensor.transpose(acc[:, 0, h, j * P:(j + 1) * P], w[:, 0, h, j * P:(j + 1) * P],
                                                      ident[:])
                    ins.then_inc(row_turned, 1)
                    pe.wait_ge(col_spread, c + 1)
                    for h in range(H):
                        for j in range(NB):
                            ins = nc.tensor.matmul(acc[:, 1, h, j * P:(j + 1) * P], w[:, 1, h, j * P:(j + 1) * P],
                                                   ident[:], start=True, stop=True)
                    ins.then_inc(row_spread, 1)

            def masked(unit, win, slot, s, t):
                pe.wait_ge(cast_done, done(NB * (win + 1)))
                pe.wait_ge(u_done, done(unit - 1))
                make_mask(slot, s, t).then_inc(mask_done, 1)

            def begin(c):
                pe.wait_ge(acc_copied, done(c - 1))
                pe.wait_ge(fin_read, done(H * (c - 1)))
                for h in range(H):
                    nc.tensor.matmul(acc[:, bass.ds(c % 2, 1), h, :], zero_bf[:, 0:P], zero_bf[:],
                                     start=True, stop=False, skip_group_check=True)
                nc.tensor.matmul(fin[:, bass.ds(c % 2, 1), DEG:CH], zero_bf[:, 0:P], zero_bf[:, 0:NB],
                                 start=True, stop=False, skip_group_check=True)

            def body(c, g, closing):
                for k in range(BODY):
                    unit = c * MT + g * BODY + k
                    if k % WT == 0:
                        pe.wait_ge(win_loaded[k // WT], 16 * (c * GC + g + 1))
                    pe.wait_ge(weight_done, done(unit + 1))
                    for h in range(H):
                        ins = nc.tensor.matmul(acc[0:F + 1, bass.ds(c % 2, 1), h, :],
                                               conv_win[:, k // WT, k % WT, h, :], u[:, k % 4, h, :],
                                               start=False, stop=False, skip_group_check=True)
                    ins.then_inc(sum_done, 1)
                    masked(unit + WT, (c * GC + g) * 2 + k // WT + 1, k % 2, (k // WT + 1) % 2, k % WT)
                    pe.wait_ge(at_done, done(unit + 1))
                    for j in range(NB):
                        ins = nc.tensor.matmul(fin[:, bass.ds(c % 2, 1), DEG + j:DEG + j + 1],
                                               at[:, k // WT, k % WT, j * P:(j + 1) * P],
                                               one_bf[:, 0:1], start=False, stop=False, skip_group_check=True)
                    ins.then_inc(deg_done, 1)
                    if closing and k in (3, 6):
                        turn(c - 1, (k - 3) // 3)

            def turn(c, h):
                pe.wait_ge(acc_copied, done(c + 1))
                pe.wait_ge(fin_read, done(H * c + h))
                pe.sem_inc(gate_pe, 1)
                for j in range(NB):
                    ins = nc.tensor.matmul(fin[:, bass.ds(c % 2, 1), j * (F + 1):(j + 1) * (F + 1)],
                                           acc_sb[:, h, j * P:(j + 1) * P], ident[0:F + 1, 0:F + 1],
                                           start=(j == 0), stop=(j == NB - 1),
                                           skip_group_check=True)
                ins.then_inc(turn_done, 1)

            def weigh():
                for k in range(WT):
                    masked(k, 0, k % 2, 0, k)
                begin(0)
                with pe.Fori(0, GC) as g:
                    body(0, g, False)
                with pe.Fori(1, NC) as c:
                    begin(c)
                    body(c, 0, True)
                    with pe.Fori(1, GC) as g:
                        body(c, g, False)
                for h in range(H):
                    turn(NC - 1, h)

            beyond = pe.value_load(flag[0:1, 0:1], min_val=0, max_val=1)
            with pe.If(beyond == 1):
                find_maxima()
            weigh()

        @block.scalar
        def _(act):
            for s in (raised_done, relu_done, exp_done, acc_copied, row_kept):
                act.sem_inc(s, PRIME)

            def find_maxima():
                with act.Fori(0, NC) as c:
                    act.wait_ge(row_spread, c + 1)
                    nc.scalar.activation(self_row[:, :, bass.ds(c * CH, CH)], acc[:, 1], ACT.Copy) \
                        .then_inc(row_kept, 1)

            def raise_(unit, slot):
                act.wait_ge(raw_done, done(unit + 1))
                nc.scalar.activation(u[:, slot], u[:, slot], ACT.Exp).then_inc(raised_done, 1)

            def relu(unit, slot):
                act.wait_ge(u_done, done(unit + 1))
                nc.scalar.activation(w[:, slot], u[:, slot], ACT.Relu, bias=1.0, scale=-1.0) \
                    .then_inc(relu_done, 1)

            def exp(unit, slot):
                act.wait_ge(relu_done, done(unit + 1))
                nc.scalar.activation(w[:, slot], w[:, slot], ACT.Exp, scale=-1.0).then_inc(exp_done, 1)

            def body(c, g, closing, general):
                for k in range(BODY):
                    unit = c * MT + g * BODY + k
                    if general:
                        raise_(unit + 2, (k + 2) % 4)
                    relu(unit + 1, (k + 1) % 4)
                    exp(unit, k % 4)
                    if closing and k == 2:
                        copy_sums(c - 1)

            def copy_sums(c):
                act.wait_ge(sum_done, done(MT * (c + 1)))
                act.wait_ge(turn_done, done(H * c))
                nc.scalar.activation(acc_sb[:].rearrange("p (a h) n -> p a h n", a=1),
                                     acc[0:F + 1, bass.ds(c % 2, 1)], ACT.Copy).then_inc(acc_copied, 1)

            def weigh(general):
                if general:
                    raise_(0, 0)
                    raise_(1, 1)
                relu(0, 0)
                with act.Fori(0, GC) as g:
                    body(0, g, False, general)
                with act.Fori(1, NC) as c:
                    body(c, 0, True, general)
                    with act.Fori(1, GC) as g:
                        body(c, g, False, general)
                copy_sums(NC - 1)

            beyond = act.value_load(flag[0:1, 0:1], min_val=0, max_val=1)
            with act.If(beyond == 1):
                find_maxima()
                weigh(True)
            with act.Else():
                weigh(False)

        @block.vector
        def _(dve):
            for s in (raw_done, u_done, weight_done, fin_read, row_max):
                dve.sem_inc(s, PRIME)

            def find_maxima():
                peak, spread = w[:, 0], w[:, 1]
                with dve.Fori(0, NC) as c:
                    steps = [0]

                    def then(ins):
                        steps[0] += 1
                        ins.then_inc(col_step, 1)
                        dve.wait_ge(col_step, c * 5 + steps[0])

                    cols = bass.ds(c * NB, NB)
                    then(nc.vector.memset(peak, -BIG))
                    dve.sem_inc(gate_dve, 1)
                    with dve.Fori(0, GC) as g:
                        for k in range(BODY):
                            unit = c * MT + g * BODY + k
                            dve.wait_ge(row_masked, done(unit + 1))
                            dve.wait_ge(row_max, done(unit))
                            for h in range(H):
                                ins = nc.vector.scalar_tensor_tensor(
                                    peak[:, h, :], mask[:, k % 2, :], score_col[:, H + h, bass.ds(g * BODY + k, 1)],
                                    peak[:, h, :], op0=ALU.add, op1=ALU.max)
                            ins.then_inc(row_max, 1)
                    dve.wait_ge(row_turned, done(c + 1))
                    then(nc.vector.tensor_reduce(row_top[:], acc[:, 0].rearrange("p h (j m) -> p h j m", j=NB),
                                                 AX_X, ALU.max))
                    then(nc.vector.tensor_tensor(row_top[:], row_top[:], score_col[:, 0:H, cols], ALU.add))
                    then(nc.vector.tensor_scalar(row_top[:], row_top[:], -2 * BOUND, 0.0, ALU.add, ALU.max))
                    then(nc.vector.tensor_tensor(row_top[:], score_col[:, 0:H, cols], row_top[:], ALU.subtract))
                    for h in range(H):
                        for j in range(NB):
                            ins = nc.vector.tensor_scalar(spread[:, h, j * P:(j + 1) * P], ones[:],
                                                          row_top[:, h, j:j + 1], None, ALU.mult)
                    ins.then_inc(col_spread, 1)
                    dve.wait_ge(row_kept, done(c + 1))

            def scores(unit, chunk, tile, k, general):
                slot = k % 4
                rows = self_row[:, :, bass.ds(chunk * CH, CH)]
                dve.wait_ge(mask_done, done(unit + 1))
                dve.wait_ge(sum_done, done(unit - 3))
                dve.wait_ge(at_done, done(unit - 3))
                if not general:
                    for h in range(H):
                        ins = nc.vector.scalar_tensor_tensor(
                            u[:, slot, h, :], rows[:, h, :], e_neigh[:, h, bass.ds(tile, 1)],
                            mask[:, k % 2, :], op0=ALU.mult, op1=ALU.add)
                    ins.then_inc(u_done, 1)
                    return
                for h in range(H):
                    ins = nc.vector.tensor_scalar(u[:, slot, h, :], rows[:, h, :],
                                                  score_col[:, H + h, bass.ds(tile, 1)], CAP, ALU.add, ALU.min)
                ins.then_inc(raw_done, 1)
                dve.wait_ge(raised_done, done(unit + 1))
                for h in range(H):
                    ins = nc.vector.tensor_tensor(u[:, slot, h, :], u[:, slot, h, :], mask[:, k % 2, :], ALU.add)
                ins.then_inc(u_done, 1)

            def body(c, g, closing, general):
                for k in range(BODY):
                    unit = c * MT + g * BODY + k
                    chunk = c if k < BODY - 2 else ((c * GC + g + 1) // GC) % NC
                    scores(unit + 2, chunk, g * BODY + k + 2, k + 2, general)
                    dve.wait_ge(exp_done, done(unit + 1))
                    nc.vector.tensor_tensor(u[:, k % 4], u[:, k % 4], w[:, k % 4], ALU.max) \
                        .then_inc(weight_done, 1)
                    if closing and k in (4, 7):
                        finish(c - 1, (k - 4) // 3)

            def finish(c, h):
                dve.wait_ge(turn_done, done(H * c + h + 1))
                if h == 0:
                    dve.wait_ge(deg_done, done(MT * (c + 1)))
                    nc.vector.tensor_copy(deg[:, bass.ds(c * NB, NB)].rearrange("p (a j) -> p a j", a=1),
                                          fin[:, bass.ds(c % 2, 1), DEG:CH])
                turned = fin[:, bass.ds(c % 2, 1), 0:FIN].rearrange("p a (j f) -> p (a j) f", f=F + 1)
                dve.sem_inc(gate_dve, 1)
                nc.vector.reciprocal(rden[:, h, :], turned[:, :, F]).then_inc(rden_done, 1)
                dve.wait_ge(rden_done, H * c + h + 1)
                for j in range(NB):
                    rows = x1[:, bass.ds(c * NB + j, 1), h * F:(h + 1) * F].rearrange("p a f -> p (a f)")
                    ins = nc.vector.scalar_tensor_tensor(rows, turned[:, j, 0:F], rden[:, h, j:j + 1], rows,
                                                         op0=ALU.mult, op1=ALU.add)
                ins.then_inc(fin_read, 1)

            def weigh(general):
                for k in range(2):
                    scores(k, 0, k, k, general)
                with dve.Fori(0, GC) as g:
                    body(0, g, False, general)
                with dve.Fori(1, NC) as c:
                    body(c, 0, True, general)
                    with dve.Fori(1, GC) as g:
                        body(c, g, False, general)
                for h in range(H):
                    finish(NC - 1, h)

            beyond = dve.value_load(flag[0:1, 0:1], min_val=0, max_val=1)
            with dve.If(beyond == 1):
                find_maxima()
                weigh(True)
            with dve.Else():
                weigh(False)


def layer1(nc, w1, b1, w2, b2, adj_t, y2_rows, x1, deg, ident, out):
    with ExitStack() as ctx:
        def sb(name, shape, dt=F32):
            return ctx.enter_context(nc.sbuf_tensor(name, shape, dt))

        col = sb("col", [P, 8, MT])
        mean, rstd, dinv, dinv_y, sq, dinv2, sim_sum, spare = (col[:, k, :] for k in range(8))
        near = sb("near", [P, MT, 8])
        near_at = sb("near_at", [P, MT, 8], U32)
        sim = sb("sim", [P, NEIGHBOURS, MT])
        tables = dict(x1=x1, deg=deg, ident=ident, mean=mean, rstd=rstd, dinv=dinv, dinv_y=dinv_y, sq=sq,
                      dinv2=dinv2, sim_sum=sim_sum, spare=spare, near=near, near_at=near_at, sim=sim)
        with nc.sbuf_tensor("z_t", [P, N], F32) as z_t, nc.sbuf_tensor("sq_parts", [P, N], BF16) as sq_parts:
            with nc.sbuf_tensor("y", [P, 2, MT, D], F16) as y:
                norm_and_scale(nc, y, **tables)
                first_product(nc, w1, b1, adj_t, y, z_t, sq_parts, **tables)
            top_k(nc, z_t, sq_parts, **tables)
        with nc.sbuf_tensor("y2", [P, 2, MT, D], F16) as y:
            similarities(nc, b2, y2_rows, y, **tables)
            second_product(nc, w2, adj_t, y2_rows, y, out, **tables)


def split_rows(nc, dve, x1, scale, y, t, done_sem):
    row = x1[:, bass.ds(t, 1), :].rearrange("p a d -> p (a d)")
    hi, lo = (y[:, k, bass.ds(t, 1), :].rearrange("p a d -> p (a d)") for k in range(2))
    return (lambda: nc.vector.tensor_scalar(hi, row, scale[:, bass.ds(t, 1)], None, ALU.mult),
            lambda: nc.vector.scalar_tensor_tensor(lo, row, scale[:, bass.ds(t, 1)], hi, op0=ALU.mult,
                                                   op1=ALU.subtract))


def norm_and_scale(nc, y, x1, deg, mean, rstd, dinv, dinv_y, **_):
    with ExitStack() as ctx:
        st = ctx.enter_context(nc.sbuf_tensor("st", [P, NB, 6], F32))
        mv = ctx.enter_context(nc.sbuf_tensor("mv", [P, NB, 2], F32))
        eps = ctx.enter_context(nc.sbuf_tensor("eps", [P, 1], F32))
        stats_done = ctx.enter_context(nc.semaphore("stats_done"))
        mv_done = ctx.enter_context(nc.semaphore("mv_done"))
        gate = ctx.enter_context(nc.semaphore("gate2"))
        var_kept = ctx.enter_context(nc.semaphore("var_kept"))
        root_done = ctx.enter_context(nc.semaphore("root_done"))
        inv_done = ctx.enter_context(nc.semaphore("inv_done"))
        norm_done = ctx.enter_context(nc.semaphore("norm_done"))
        hi_done = ctx.enter_context(nc.semaphore("hi_done"))
        eps_made = ctx.enter_context(nc.semaphore("eps_made"))
        block = ctx.enter_context(nc.Block())

        @block.scalar
        def _(act):
            act.wait_ge(eps_made, 1)
            act.wait_ge(var_kept, NC)
            nc.scalar.activation(rstd, rstd, ACT.Sqrt, bias=eps[:]).then_inc(root_done, 1)
            nc.scalar.activation(dinv, deg[:], ACT.Sqrt).then_inc(root_done, 1)

        @block.vector
        def _(dve):
            nc.vector.memset(eps[:], EPS_LN).then_inc(eps_made, 1)
            with dve.Fori(0, NC) as c:
                for j in range(NB):
                    ins = nc.vector.bn_stats(st[:, j, :], x1[:, bass.ds(c * NB + j, 1), :])
                ins.then_inc(stats_done, 1)
                dve.wait_ge(stats_done, c + 1)
                dve.sem_inc(gate, 1)
                for j in range(NB):
                    ins = nc.vector.bn_aggr(mv[:, j, :], st[:, j, :])
                ins.then_inc(mv_done, 1)
                dve.wait_ge(mv_done, c + 1)
                nc.vector.tensor_copy(mean[:, bass.ds(c * NB, NB)], mv[:, :, 0])
                nc.vector.tensor_copy(rstd[:, bass.ds(c * NB, NB)], mv[:, :, 1]).then_inc(var_kept, 1)
                dve.wait_ge(var_kept, c + 1)
            dve.wait_ge(root_done, 2)
            nc.vector.reciprocal(rstd, rstd).then_inc(inv_done, 1)
            nc.vector.reciprocal(dinv, dinv).then_inc(inv_done, 1)
            dve.wait_ge(inv_done, 2)
            nc.vector.tensor_scalar(dinv_y, dinv, YSCALE, None, ALU.mult).then_inc(inv_done, 1)
            dve.wait_ge(inv_done, 3)
            with dve.Fori(0, NC) as c:
                for j in range(NB):
                    t = c * NB + j
                    row = x1[:, bass.ds(t, 1), :]
                    nc.vector.tensor_scalar(row, row, mean[:, bass.ds(t, 1)], rstd[:, bass.ds(t, 1)],
                                            ALU.subtract, ALU.mult).then_inc(norm_done, 1)
                dve.wait_ge(norm_done, c * NB + NB)
                parts = [split_rows(nc, dve, x1, dinv_y, y, c * NB + j, hi_done) for j in range(NB)]
                for hi, _ in parts:
                    hi().then_inc(hi_done, 1)
                dve.wait_ge(hi_done, c * NB + NB)
                for _, lo in parts:
                    lo()


def load_adj_t(nc, sp, adj_t, at, at_loaded, at_used):
    with sp.Fori(0, NC * NLW // 4) as g:
        for s in range(4):
            win = g * 4 + s
            sp.wait_ge(at_used, done(win - 3))
            sp.dma_start(at[:, s], adj_t[win // NLW, :, bass.ds((win % NLW) * LW, LW), :]) \
                .then_inc(at_loaded[s], 16)


def adj_product(nc, pe, c, agg, at, y, at_loaded, at_used, zero):
    nc.tensor.matmul(agg, zero[:, 0:P], zero[:], start=True, stop=False, skip_group_check=True)
    with pe.Fori(0, NLW // 4) as g:
        for s in range(4):
            pe.wait_ge(at_loaded[s], (c * (NLW // 4) + g + 1) * 16)
            for t in range(LW):
                for part in range(2):
                    rows = y[:, part, bass.ds((g * 4 + s) * LW + t, 1), :].rearrange("p a d -> p (a d)")
                    ins = nc.tensor.matmul(agg, rows, at[:, s, t, :], start=False, stop=False,
                                           skip_group_check=True)
            ins.then_inc(at_used, 1)


def first_product(nc, w1, b1, adj_t, y, z_t, sq_parts, ident, dinv, sq, **_):
    with ExitStack() as ctx:
        def sb(name, shape, dt=F32):
            return ctx.enter_context(nc.sbuf_tensor(name, shape, dt))

        def psum(name, shape):
            return ctx.enter_context(nc.psum_tensor(name, shape, F32))

        def sem(name):
            return ctx.enter_context(nc.semaphore(name))

        at = sb("at_in", [P, 4, LW, CH], BF16)
        zero = sb("zero", [P, CH], BF16)
        ones = sb("ones1", [P, P])
        w1_sb = sb("w1_sb", [D, D])
        b1_sb = sb("b1_sb", [D, 1])
        agg_sb = sb("agg_sb", [D, CH])
        dinv_b = sb("dinv_b", [P, NB, P])
        dinv_row = sb("dinv_row", [P, CH])
        zsq = sb("zsq", [D, CH])
        half = sb("half", [P, CH])
        rest = sb("rest", [P, CH])
        part = sb("part", [P, 3, CH], BF16)
        agg = psum("agg", [P, 2, CH])
        zp = psum("zp", [P, CH])
        dp = psum("dp", [P, CH])
        sp_row = psum("sp_row", [P, CH])
        sp_col = psum("sp_col", [P, NB])

        w_loaded = sem("w_loaded")
        made = sem("made")
        at_loaded = [sem(f"at_loaded{s}") for s in range(4)]
        at_used = sem("at_used")
        agg_done = sem("agg_done")
        agg_kept = sem("agg_kept")
        dinv_b_done = sem("dinv_b_done")
        z_raw_done = sem("z_raw_done")
        row_kept = sem("row_kept")
        z_step = sem("z_step")
        zsq_done = sem("zsq_done")
        sq_done = sem("sq_done")
        chunk_done = sem("chunk_done1")
        block = ctx.enter_context(nc.Block())

        @block.sync
        def _(sp):
            sp.dma_start(w1_sb[:], w1).then_inc(w_loaded, 16)
            sp.dma_start(b1_sb[:], b1.rearrange("(d a) -> d a", a=1)).then_inc(w_loaded, 16)
            load_adj_t(nc, sp, adj_t, at, at_loaded, at_used)

        @block.gpsimd
        def _(pool):
            nc.gpsimd.memset(zero[:], 0.0).then_inc(made, 1)
            nc.gpsimd.memset(ones[:], 1.0).then_inc(made, 1)
            nc.gpsimd.memset(sq_parts[:], 0.0).then_inc(made, 1)

        @block.tensor
        def _(pe):
            for s in (at_used, agg_done):
                pe.sem_inc(s, PRIME)
            pe.wait_ge(made, 3)
            pe.wait_ge(w_loaded, 32)

            def finish(c, s):
                pe.wait_ge(agg_kept, c + 1)
                pe.wait_ge(chunk_done, done(c))
                nc.tensor.matmul(zp[:], w1_sb[:], agg_sb[:], start=True, stop=True)
                pe.wait_ge(dinv_b_done, c + 1)
                for j in range(NB):
                    ins = nc.tensor.matmul(dp[:, j * P:(j + 1) * P], dinv_b[:, j, :], ident[:],
                                           start=True, stop=True)
                ins.then_inc(z_raw_done, 1)

            def squares(c):
                pe.wait_ge(zsq_done, c + 1)
                nc.tensor.matmul(sp_row[:], ones[:], zsq[:], start=True, stop=True)
                for j in range(NB):
                    ins = nc.tensor.matmul(sp_col[:, j:j + 1], zsq[:, j * P:(j + 1) * P], ones[:, 0:1],
                                           start=True, stop=True)
                ins.then_inc(sq_done, 1)

            with pe.Fori(0, NC // 2) as g2:
                for s in range(2):
                    c = g2 * 2 + s
                    adj_product(nc, pe, c, agg[:, s, :], at, y, at_loaded, at_used, zero)
                    nc.tensor.matmul(agg[:, s, :], zero[:, 0:P], zero[:], start=False, stop=True,
                                     skip_group_check=True).then_inc(agg_done, 1)
                    finish(c, s)
                    squares(c)

        @block.scalar
        def _(act):
            with act.Fori(0, NC // 2) as g2:
                for s in range(2):
                    c = g2 * 2 + s
                    act.wait_ge(agg_done, done(c + 1))
                    act.wait_ge(chunk_done, done(c))
                    nc.scalar.activation(agg_sb[:], agg[:, s, :], ACT.Copy, scale=1.0 / YSCALE) \
                        .then_inc(agg_kept, 1)
                    act.wait_ge(z_raw_done, c + 1)
                    nc.scalar.activation(dinv_row[:], dp[:], ACT.Copy).then_inc(row_kept, 1)

        @block.vector
        def _(dve):
            dve.sem_inc(chunk_done, PRIME)
            dve.wait_ge(made, 3)
            dve.wait_ge(w_loaded, 32)
            STEPS = 8
            with dve.Fori(0, NC) as c:
                cols = bass.ds(c * CH, CH)
                zc = z_t[:, cols]
                k = [0]

                def then(ins):
                    k[0] += 1
                    ins.then_inc(z_step, 1)
                    dve.wait_ge(z_step, c * STEPS + k[0])

                for j in range(NB):
                    ins = nc.vector.tensor_scalar(dinv_b[:, j, :], ones[:], dinv[:, bass.ds(c * NB + j, 1)], None,
                                                  ALU.mult)
                ins.then_inc(dinv_b_done, 1)
                dve.wait_ge(row_kept, c + 1)
                then(nc.vector.tensor_tensor(zc, zp[:], dinv_row[:], ALU.mult))
                then(nc.vector.tensor_scalar(zc, zc, b1_sb[:], None, ALU.add))
                then(nc.vector.scalar_tensor_tensor(zc, zc, SLOPE, zc, op0=ALU.mult, op1=ALU.max))
                nc.vector.tensor_tensor(zsq[:], zc, zc, ALU.mult).then_inc(zsq_done, 1)
                dve.wait_ge(sq_done, c + 1)
                nc.vector.tensor_copy(sq[:, bass.ds(c * NB, NB)], sp_col[:])
                then(nc.vector.tensor_scalar(half[:], sp_row[:], -0.5, None, ALU.mult))
                then(nc.vector.tensor_copy(part[:, 0, :], half[:]))
                then(nc.vector.tensor_tensor(rest[:], half[:], part[:, 0, :], ALU.subtract))
                then(nc.vector.tensor_copy(part[:, 1, :], rest[:]))
                then(nc.vector.tensor_tensor(part[:, 2, :], rest[:], part[:, 1, :], ALU.subtract))
                assert k[0] == STEPS
                for q in range(3):
                    ins = nc.vector.tensor_copy(sq_parts[32 * q:32 * q + 1, cols], part[32 * q:32 * q + 1, q, :])
                ins.then_inc(chunk_done, 1)
                dve.wait_ge(chunk_done, done(c + 1))


def top_k(nc, z_t, sq_parts, near, near_at, **_):
    GROUP = 2
    NG = NC // GROUP
    with ExitStack() as ctx:
        g_sb = ctx.enter_context(nc.sbuf_tensor("g_sb", [P, 2, N], F32))
        z_blk = ctx.enter_context(nc.sbuf_tensor("z_blk", [P, 2, P], F32))
        pick = ctx.enter_context(nc.sbuf_tensor("pick", [P, P], BF16))
        prod = ctx.enter_context(nc.psum_tensor("prod_ps", [P, 4, GROUP, CH], F32))
        made = ctx.enter_context(nc.semaphore("pick_made"))
        blk_done = ctx.enter_context(nc.semaphore("blk_done"))
        prod_done = ctx.enter_context(nc.semaphore("prod_done"))
        g_kept = ctx.enter_context(nc.semaphore("g_kept"))
        best = ctx.enter_context(nc.sbuf_tensor("best", [P, 2, 8], F32))
        best_at = ctx.enter_context(nc.sbuf_tensor("best_at", [P, 2, 8], U32))
        gate = ctx.enter_context(nc.semaphore("gate5"))
        max_done = ctx.enter_context(nc.semaphore("max_done"))
        kept_done = ctx.enter_context(nc.semaphore("kept_done"))
        at_done = ctx.enter_context(nc.semaphore("index_done"))
        block = ctx.enter_context(nc.Block())

        @block.gpsimd
        def _(pool):
            nc.gpsimd.memset(pick[:], 0.0).then_inc(made, 1)
            pool.wait_ge(made, 1)
            for q in range(3):
                ins = nc.gpsimd.memset(pick[32 * q:32 * q + 1, :], 1.0)
            ins.then_inc(made, 1)
            pool.wait_ge(made, 2)
            pool.sem_inc(blk_done, PRIME)
            with pool.Fori(0, MT // 2) as g:
                for s in range(2):
                    t = g * 2 + s
                    pool.wait_ge(prod_done, done(NG * (t - 1)))
                    nc.gpsimd.tensor_copy(z_blk[:, s, :], z_t[:, bass.ds(t * P, P)]).then_inc(blk_done, 1)

        @block.tensor
        def _(pe):
            pe.sem_inc(prod_done, PRIME)
            pe.wait_ge(made, 2)
            with pe.Fori(0, MT // 2) as g:
                for s in range(2):
                    t = g * 2 + s
                    pe.wait_ge(blk_done, done(t + 1))
                    for q in range(NG):
                        pe.wait_ge(g_kept, done(NG * t + q - 3))
                        for b in range(GROUP):
                            m = (q * GROUP + b) * CH
                            bank = prod[:, q % 4, b, :]
                            nc.tensor.matmul(bank, pick[:], sq_parts[:, m:m + CH], start=True, stop=False)
                            ins = nc.tensor.matmul(bank, z_blk[:, s, :], z_t[:, m:m + CH], start=False, stop=True)
                        ins.then_inc(prod_done, 1)

        @block.scalar
        def _(act):
            act.sem_inc(g_kept, PRIME)
            with act.Fori(0, MT // 2) as g:
                for s in range(2):
                    t = g * 2 + s
                    act.wait_ge(at_done, done(t - 1))
                    for q in range(NG):
                        act.wait_ge(prod_done, done(NG * t + q + 1))
                        nc.scalar.activation(g_sb[:, s, q * GROUP * CH:(q + 1) * GROUP * CH]
                                             .rearrange("p (b m) -> p b m", b=GROUP),
                                             prod[:, q % 4], ACT.Copy).then_inc(g_kept, 1)

        @block.vector
        def _(dve):
            dve.sem_inc(at_done, PRIME)
            with dve.Fori(0, MT // 2) as g:
                for s in range(2):
                    t = g * 2 + s
                    dve.wait_ge(g_kept, done(NG * (t + 1)))
                    dve.sem_inc(gate, 1)
                    nc.vector.max(best[:, s], g_sb[:, s, :]).then_inc(max_done, 1)
                    dve.wait_ge(max_done, t + 1)
                    dve.sem_inc(gate, 1)
                    nc.vector.max_index(best_at[:, s], best[:, s], g_sb[:, s, :]).then_inc(at_done, 1)
                    nc.vector.tensor_copy(near[:, bass.ds(t, 1), :].rearrange("p a k -> p (a k)"), best[:, s])
                    dve.wait_ge(at_done, done(t + 1))
                    nc.vector.tensor_copy(near_at[:, bass.ds(t, 1), :].rearrange("p a k -> p (a k)"), best_at[:, s]) \
                        .then_inc(kept_done, 1)
                    dve.wait_ge(kept_done, t + 1)


def similarities(nc, b2, y2_rows, y, x1, deg, sq, dinv, dinv_y, dinv2, sim_sum, near, sim, spare, **_):
    with ExitStack() as ctx:
        y_f = ctx.enter_context(nc.sbuf_tensor("y_f", [P, MT, D], F32))
        b2_row = ctx.enter_context(nc.sbuf_tensor("b2_row", [1, D], F32))
        b2_all = ctx.enter_context(nc.sbuf_tensor("b2_all", [P, D], F32))
        ones = ctx.enter_context(nc.sbuf_tensor("ones2", [1, P], F32))
        eps = ctx.enter_context(nc.sbuf_tensor("eps_d2", [P, 1], F32))
        b2_ps = ctx.enter_context(nc.psum_tensor("b2_ps", [P, D], F32))
        b2_loaded = ctx.enter_context(nc.semaphore("b2_loaded"))
        ones_made = ctx.enter_context(nc.semaphore("ones_made"))
        b2_spread = ctx.enter_context(nc.semaphore("b2_spread"))
        d2_done = ctx.enter_context(nc.semaphore("d2_done"))
        sim_done = ctx.enter_context(nc.semaphore("sim_done"))
        step = ctx.enter_context(nc.semaphore("step2"))
        root2_done = ctx.enter_context(nc.semaphore("root2_done"))
        dist_done = ctx.enter_context(nc.semaphore("dist_done"))
        y_done = ctx.enter_context(nc.semaphore("y_done"))
        hi_done = ctx.enter_context(nc.semaphore("hi2_done"))
        y_stored = ctx.enter_context(nc.semaphore("y_stored"))
        block = ctx.enter_context(nc.Block())

        @block.sync
        def _(sp):
            sp.dma_start(b2_row[:], b2.rearrange("(a d) -> a d", a=1)).then_inc(b2_loaded, 16)
            sp.wait_ge(y_done, MT)
            sp.dma_start(y2_rows.rearrange("(t p) d -> p t d", p=P), y_f[:]).then_inc(y_stored, 16)
            sp.wait_ge(y_stored, 16)

        @block.tensor
        def _(pe):
            pe.wait_ge(b2_loaded, 16)
            pe.wait_ge(ones_made, 2)
            nc.tensor.matmul(b2_ps[:], ones[:], b2_row[:], start=True, stop=True).then_inc(b2_spread, 1)

        @block.scalar
        def _(act):
            act.wait_ge(d2_done, 1)
            act.wait_ge(ones_made, 2)
            nc.scalar.activation(sim[:], sim[:], ACT.Sqrt, bias=eps[:]).then_inc(dist_done, 1)
            act.wait_ge(dist_done, 1)
            nc.scalar.activation(sim[:], sim[:], ACT.Exp, scale=-0.5).then_inc(sim_done, 1)
            act.wait_ge(step, 3)
            nc.scalar.activation(dinv2, sim_sum, ACT.Sqrt).then_inc(root2_done, 1)

        @block.vector
        def _(dve):
            nc.vector.memset(ones[:], 1.0).then_inc(ones_made, 1)
            nc.vector.memset(eps[:], EPS_D2).then_inc(ones_made, 1)
            for k in range(NEIGHBOURS):
                ins = nc.vector.scalar_tensor_tensor(sim[:, k, :], near[:, :, k], -2.0, sq, op0=ALU.mult, op1=ALU.add)
            ins.then_inc(step, 1)
            dve.wait_ge(step, 1)
            nc.vector.tensor_scalar(sim[:], sim[:], 0.0, None, ALU.max).then_inc(d2_done, 1)
            dve.wait_ge(sim_done, 1)
            nc.vector.tensor_reduce(spare, sim[:].rearrange("p k t -> p t k"), AX_X, ALU.add).then_inc(step, 1)
            dve.wait_ge(step, 2)
            nc.vector.tensor_tensor(sim_sum, spare, deg[:], ALU.add).then_inc(step, 1)
            dve.wait_ge(root2_done, 1)
            nc.vector.reciprocal(dinv2, dinv2).then_inc(step, 1)
            dve.wait_ge(step, 4)
            nc.vector.tensor_scalar(dinv_y, dinv2, YSCALE, None, ALU.mult).then_inc(step, 1)
            dve.wait_ge(step, 5)
            nc.vector.tensor_scalar(sim[:], sim[:], YSCALE, None, ALU.mult).then_inc(step, 1)
            dve.wait_ge(b2_spread, 1)
            nc.vector.tensor_copy(b2_all[:], b2_ps[:]).then_inc(step, 1)
            dve.wait_ge(step, 7)
            with dve.Fori(0, NC) as c:
                parts = [split_rows(nc, dve, x1, dinv_y, y, c * NB + j, hi_done) for j in range(NB)]
                for j, (hi, _) in enumerate(parts):
                    t = c * NB + j
                    nc.vector.tensor_scalar(y_f[:, bass.ds(t, 1), :], x1[:, bass.ds(t, 1), :],
                                            dinv2[:, bass.ds(t, 1)], None, ALU.mult).then_inc(y_done, 1)
                    hi().then_inc(hi_done, 1)
                dve.wait_ge(hi_done, c * 2 * NB + NB)
                for _, lo in parts:
                    lo().then_inc(hi_done, 1)
                dve.wait_ge(hi_done, c * 2 * NB + 2 * NB)
                for j in range(NB):
                    row = x1[:, bass.ds(c * NB + j, 1), :].rearrange("p a d -> p (a d)")
                    nc.vector.tensor_tensor(row, row, b2_all[:], ALU.add)


def second_product(nc, w2, adj_t, y2_rows, y, out, x1, ident, dinv2, near_at, sim, **_):
    with ExitStack() as ctx:
        def sb(name, shape, dt=F32):
            return ctx.enter_context(nc.sbuf_tensor(name, shape, dt))

        def psum(name, shape):
            return ctx.enter_context(nc.psum_tensor(name, shape, F32))

        def sem(name):
            return ctx.enter_context(nc.semaphore(name))

        at = sb("at_in2", [P, 4, LW, CH], BF16)
        zero = sb("zero2", [P, CH], BF16)
        w2_sb = sb("w2_sb", [D, D])
        at_rows = sb("at_rows", [P, 2, NB, NEIGHBOURS], U32)
        near_y = sb("near_y", [P, 2, NB, NEIGHBOURS, D])
        near_sum = sb("near_sum", [P, 2, NB, D])
        agg_sb = sb("agg_sb2", [D, CH])
        h = sb("h", [P, 2, NB, D])
        st = sb("st2", [P, NB, 6])
        mv = sb("mv2", [P, NB, 2])
        rs = sb("rs", [P, NB])
        eps = sb("eps2", [P, 1])
        agg = psum("agg2", [P, 2, CH])
        op = psum("op", [P, 2, NB, D])

        w_loaded = sem("w2_loaded")
        made = sem("made2")
        at_loaded = [sem(f"at2_loaded{s}") for s in range(4)]
        at_used = sem("at2_used")
        index_kept = sem("index_kept")
        gate = sem("gate3")
        near_loaded = [sem("near_loaded0"), sem("near_loaded1")]
        near_step = sem("near_step")
        gate_dve = sem("gate4")
        near_summed = sem("near_summed")
        agg_done = sem("agg2_done")
        agg_kept = sem("agg2_kept")
        op_done = sem("op_done")
        h_step = sem("h_step")
        var_done = sem("var_done")
        root_done = sem("root3_done")
        h_done = sem("h_done")
        stored = [sem("stored0"), sem("stored1")]
        out_view = out.rearrange("(c j p) d -> c p j d", j=NB, p=P)
        block = ctx.enter_context(nc.Block())

        @block.sync
        def _(sp):
            sp.dma_start(w2_sb[:], w2).then_inc(w_loaded, 16)
            load_adj_t(nc, sp, adj_t, at, at_loaded, at_used)

        @block.gpsimd
        def _(pool):
            nc.gpsimd.memset(zero[:], 0.0).then_inc(made, 1)
            nc.gpsimd.memset(eps[:], EPS_LN).then_inc(made, 1)
            pool.sem_inc(index_kept, PRIME)
            with pool.Fori(0, NC // 2) as g:
                for s in range(2):
                    c = g * 2 + s
                    pool.wait_ge(near_summed, done(c - 1))
                    nc.gpsimd.tensor_copy(at_rows[:, s], near_at[:, bass.ds(c * NB, NB), 0:NEIGHBOURS]) \
                        .then_inc(index_kept, 1)
                    pool.wait_ge(index_kept, done(c + 1))
                    pool.sem_inc(gate, 1)
                    for j in range(NB):
                        for k in range(NEIGHBOURS):
                            pool.indirect_dma_start(
                                out=near_y[:, s, j, k, :], out_offset=None, in_=y2_rows,
                                in_offset=bass.IndirectOffsetOnAxis(ap=at_rows[:, s, j, k:k + 1], axis=0),
                            ).then_inc(near_loaded[s], 16)

        @block.tensor
        def _(pe):
            for s in (at_used, agg_done):
                pe.sem_inc(s, PRIME)
            pe.wait_ge(made, 2)
            pe.wait_ge(w_loaded, 16)
            with pe.Fori(0, NC // 2) as g2:
                for s in range(2):
                    c = g2 * 2 + s
                    adj_product(nc, pe, c, agg[:, s, :], at, y, at_loaded, at_used, zero)
                    pe.wait_ge(near_summed, done(c + 1))
                    for j in range(NB):
                        ins = nc.tensor.matmul(agg[:, s, j * P:(j + 1) * P], near_sum[:, s, j, :], ident[:],
                                               start=False, stop=(j == NB - 1), skip_group_check=True)
                    ins.then_inc(agg_done, 1)
                    pe.wait_ge(agg_kept, c + 1)
                    pe.wait_ge(h_done, done(c - 1))
                    for j in range(NB):
                        ins = nc.tensor.matmul(op[:, s, j, :], agg_sb[:, j * P:(j + 1) * P], w2_sb[:],
                                               start=True, stop=True)
                    ins.then_inc(op_done, 1)

        @block.scalar
        def _(act):
            act.sem_inc(op_done, PRIME)
            for q in stored:
                act.sem_inc(q, 16)
            act.wait_ge(made, 2)
            with act.Fori(0, NC // 2) as g2:
                for s in range(2):
                    c = g2 * 2 + s
                    act.wait_ge(agg_done, done(c + 1))
                    act.wait_ge(op_done, done(c))
                    nc.scalar.activation(agg_sb[:], agg[:, s, :], ACT.Copy, scale=1.0 / YSCALE) \
                        .then_inc(agg_kept, 1)
                    act.wait_ge(var_done, c + 1)
                    nc.scalar.activation(rs[:], mv[:, :, 1], ACT.Sqrt, bias=eps[:]).then_inc(root_done, 1)
                    act.wait_ge(h_done, done(c + 1))
                    act.dma_start(out_view[c], h[:, s]).then_inc(stored[s], 16)
            for q in stored:
                act.wait_ge(q, 16 * (NC // 2 + 1))

        @block.vector
        def _(dve):
            for s in (near_summed, h_done):
                dve.sem_inc(s, PRIME)
            with dve.Fori(0, NC // 2) as g2:
                for s in range(2):
                    c = g2 * 2 + s
                    dve.wait_ge(near_loaded[s], 16 * NB * NEIGHBOURS * (g2 + 1))
                    dve.wait_ge(agg_done, done(c - 1))
                    for k in range(NEIGHBOURS):
                        for j in range(NB):
                            rows, total = near_y[:, s, j, k, :], near_sum[:, s, j, :]
                            weight = sim[:, k, bass.ds(c * NB + j, 1)]
                            if k == 0:
                                ins = nc.vector.tensor_scalar(total, rows, weight, None, ALU.mult)
                            else:
                                ins = nc.vector.scalar_tensor_tensor(total, rows, weight, total, op0=ALU.mult,
                                                                     op1=ALU.add)
                        if k < NEIGHBOURS - 1:
                            ins.then_inc(near_step, 1)
                            dve.wait_ge(near_step, c * (NEIGHBOURS - 1) + k + 1)
                    ins.then_inc(near_summed, 1)
                    dve.wait_ge(op_done, done(c + 1))
                    dve.wait_ge(stored[s], 16 * (g2 + 1))
                    for j in range(NB):
                        ins = nc.vector.scalar_tensor_tensor(
                            h[:, s, j, :], op[:, s, j, :], dinv2[:, bass.ds(c * NB + j, 1)],
                            x1[:, bass.ds(c * NB + j, 1), :].rearrange("p a d -> p (a d)"),
                            op0=ALU.mult, op1=ALU.add)
                    ins.then_inc(h_step, 1)
                    dve.wait_ge(h_step, c * 3 + 1)
                    for j in range(NB):
                        ins = nc.vector.bn_stats(st[:, j, :], h[:, s, j, :])
                    ins.then_inc(h_step, 1)
                    dve.wait_ge(h_step, c * 3 + 2)
                    dve.sem_inc(gate_dve, 1)
                    for j in range(NB):
                        ins = nc.vector.bn_aggr(mv[:, j, :], st[:, j, :])
                    ins.then_inc(var_done, 1)
                    dve.wait_ge(root_done, c + 1)
                    nc.vector.reciprocal(rs[:], rs[:]).then_inc(h_step, 1)
                    dve.wait_ge(h_step, c * 3 + 3)
                    for j in range(NB):
                        ins = nc.vector.tensor_scalar(h[:, s, j, :], h[:, s, j, :], mv[:, j, 0:1], rs[:, j:j + 1],
                                                      ALU.subtract, ALU.mult)
                    ins.then_inc(h_done, 1)
                    dve.wait_ge(h_done, done(c + 1))


_INS = ["x", "adj", "L0_gnn_kernels", "L0_gnn_att_kernels", "L1_gnn_W1", "L1_gnn_b1", "L1_gnn_W2", "L1_gnn_b2"]


def kernel(**inputs):
    import numpy as _np
    import concourse.bacc as _bacc
    from concourse import mybir as _mybir
    from concourse.bass_utils import run_bass_kernel_spmd as _run

    nc = _bacc.Bacc("TRN2", target_bir_lowering=False, num_devices=1)
    arrays, args = {}, []
    for name in _INS:
        a = _np.ascontiguousarray(inputs[name])
        arrays[f"in_{name}_dram"] = a
        args.append(nc.dram_tensor(f"in_{name}_dram", a.shape, _mybir.dt.from_np(a.dtype), kind="ExternalInput").ap())
    res = nc.dram_tensor("out_dram", (8192, 128), _mybir.dt.float32, kind="ExternalOutput").ap()
    resnorm_gnn_kernel(nc, *args, res)
    r = _run(nc, [arrays], core_ids=[0])
    return r.results[0]["out_dram"]
```
